# Optimizing a Trainium2 kernel written in Bass

```python
import numpy as np
import jax
import jax.numpy as jnp

def _softmax(x, axis=-1):
    return jax.nn.softmax(x, axis=axis)

def _gelu(x):
    return jax.nn.gelu(x, approximate=True)

def _silu(x):
    return jax.nn.silu(x)

def _sigmoid(x):
    return jax.nn.sigmoid(x)

def _layernorm(x, axis=-1, eps=1e-05):
    m = jnp.mean(x, axis=axis, keepdims=True)
    v = jnp.var(x, axis=axis, keepdims=True)
    return (x - m) / jnp.sqrt(v + eps)

def _scatter_add(tgt, idx, src, axis=0):
    return tgt.at[idx].add(src)

def _segment_sum(src, seg, n):
    return jax.ops.segment_sum(src, seg, n)
kernel_name = 'mk_gnn_ffn_d1_gnn_r8_d35bf4'

def setup_inputs(seed: int=0):
    np.random.seed(seed)
    _w = jnp.asarray

    def _rec_inputs():
        import jax
        import jax.numpy as jnp
        _gk = jax.random.key(seed)
        x = -0.0002117 + 1 * jax.random.normal(jax.random.fold_in(_gk, 1), (6250, 256), jnp.float32)
        src = jax.random.randint(jax.random.fold_in(_gk, 2), (100000,), 0, 6250, jnp.int32)
        dst = jax.random.randint(jax.random.fold_in(_gk, 3), (100000,), 0, 6250, jnp.int32)
        _o = jnp.argsort(dst, stable=True)
        src = src[_o]
        dst = dst[_o]
        edge_weight = jax.random.uniform(jax.random.fold_in(_gk, 12), (100000,), jnp.float32, 0.0, 0.999999)
        return (x, src, dst, edge_weight)
    x, src, dst, edge_weight = _rec_inputs()

    def _L0_gnn_setup():
        import jax, jax.numpy as jnp
        import numpy as np
        N_NODES = 12500
        N_EDGES = 200000
        D = 256
        key = jax.random.key(seed)
        ks = jax.random.split(key, 8)
        h6_all = jax.random.normal(ks[0], (N_NODES, D), dtype=jnp.float32)
        edge_index = jax.random.randint(ks[1], (2, N_EDGES), 0, N_NODES, dtype=jnp.int64)
        edge_weight = jax.random.uniform(ks[2], (N_EDGES,), dtype=jnp.float32)
        s = 1.0 / np.sqrt(D)
        W = jax.random.normal(ks[3], (D, D), dtype=jnp.float32) * s
        b = jnp.zeros((D,), dtype=jnp.float32)
        W1 = jax.random.normal(ks[4], (D, D), dtype=jnp.float32) * s
        b1 = jnp.zeros((D,), dtype=jnp.float32)
        W2 = jax.random.normal(ks[5], (D, D), dtype=jnp.float32) * s
        b2 = jnp.zeros((D,), dtype=jnp.float32)
        return {'h6_all': h6_all, 'edge_index': edge_index, 'edge_weight': edge_weight, 'W': W, 'b': b, 'W1': W1, 'b1': b1, 'W2': W2, 'b2': b2}
    _L0_gnn_all = _L0_gnn_setup()
    _L0_gnn_in = {k: v for k, v in _L0_gnn_all.items() if k in ('W', 'b', 'W1', 'b1', 'W2', 'b2')}
    del _L0_gnn_all

    def _L0_ffn_setup():
        import jax, jax.numpy as jnp
        import numpy as np
        NUM_EXPERTS = 8
        TOP_K = 2
        B, S, D = (8, 1024, 256)

        def _moe(tokens, router_w, w1, b1, w2, b2):
            N = tokens.shape[0]
            E = router_w.shape[0]
            logits = tokens.astype(jnp.float32) @ router_w.astype(jnp.float32).T
            probs = jax.nn.softmax(logits, axis=-1)
            rw, re = jax.lax.top_k(probs, TOP_K)
            if TOP_K > 1:
                rw = rw / jnp.maximum(rw.sum(-1, keepdims=True), 1e-12)
            rw = rw.astype(tokens.dtype)
            combine = jnp.zeros((N, E), tokens.dtype).at[jnp.arange(N)[:, None], re].set(rw)
            out = tokens
            for e in range(E):
                h = jax.nn.gelu(tokens @ w1[e] + b1[e], approximate=False)
                y = h @ w2[e] + b2[e]
                out = out + combine[:, e:e + 1] * y
            return out
        key = jax.random.key(seed)
        ks = jax.random.split(key, 4)
        scale = 1.0 / np.sqrt(D).astype(np.float32)
        return {'input_embeddings': jax.random.normal(ks[0], (B, S, D), jnp.float32), 'router_w': jax.random.normal(ks[1], (NUM_EXPERTS, D), jnp.float32) * scale, 'w1': jax.random.normal(ks[2], (NUM_EXPERTS, D, D), jnp.float32) * scale, 'b1': jnp.zeros((NUM_EXPERTS, D), jnp.float32), 'w2': jax.random.normal(ks[3], (NUM_EXPERTS, D, D), jnp.float32) * scale, 'b2': jnp.zeros((NUM_EXPERTS, D), jnp.float32)}
    _L0_ffn_all = _L0_ffn_setup()
    _L0_ffn_in = {k: v for k, v in _L0_ffn_all.items() if k in ('router_w', 'w1', 'b1', 'w2', 'b2')}
    del _L0_ffn_all
    return {'x': x, 'src': src, 'dst': dst, 'edge_weight': edge_weight, 'L0_gnn_W': _L0_gnn_in['W'], 'L0_gnn_b': _L0_gnn_in['b'], 'L0_gnn_W1': _L0_gnn_in['W1'], 'L0_gnn_b1': _L0_gnn_in['b1'], 'L0_gnn_W2': _L0_gnn_in['W2'], 'L0_gnn_b2': _L0_gnn_in['b2'], 'L0_ffn_router_w': _L0_ffn_in['router_w'], 'L0_ffn_w1': _L0_ffn_in['w1'], 'L0_ffn_b1': _L0_ffn_in['b1'], 'L0_ffn_w2': _L0_ffn_in['w2'], 'L0_ffn_b2': _L0_ffn_in['b2']}

def reference(x, src, dst, edge_weight, L0_gnn_W, L0_gnn_b, L0_gnn_W1, L0_gnn_b1, L0_gnn_W2, L0_gnn_b2, L0_ffn_router_w, L0_ffn_w1, L0_ffn_b1, L0_ffn_w2, L0_ffn_b2):
    import jax
    import jax.numpy as jnp

    def _L0_gnn_ref(h6_all, edge_index, edge_weight, W, b, W1, b1, W2, b2):
        import jax, jax.numpy as jnp
        import numpy as np
        N_NODES = 12500
        N_EDGES = 200000
        D = 256
        'GCNConv(256->256, weighted, self-loops, symmetric norm) + 2-layer MLP head.'
        N = h6_all.shape[0]
        row, col = (edge_index[0], edge_index[1])
        sl = jnp.arange(N, dtype=edge_index.dtype)
        row_sl = jnp.concatenate([row, sl])
        col_sl = jnp.concatenate([col, sl])
        ew_sl = jnp.concatenate([edge_weight, jnp.ones((N,), dtype=edge_weight.dtype)])
        deg = jax.ops.segment_sum(ew_sl, row_sl, num_segments=N)
        dinv = jnp.where(deg > 0, jax.lax.rsqrt(deg), 0.0)
        norm = dinv[row_sl] * ew_sl * dinv[col_sl]
        xw = h6_all @ W
        msgs = xw[col_sl] * norm[:, None]
        h7 = jax.ops.segment_sum(msgs, row_sl, num_segments=N) + b
        h = jax.nn.relu(h7 @ W1 + b1)
        out = h @ W2 + b2
        return out

    def _L0_ffn_ref(input_embeddings, router_w, w1, b1, w2, b2):
        import jax, jax.numpy as jnp
        import numpy as np
        NUM_EXPERTS = 8
        TOP_K = 2
        B, S, D = (8, 1024, 256)

        def _moe(tokens, router_w, w1, b1, w2, b2):
            N = tokens.shape[0]
            E = router_w.shape[0]
            logits = tokens.astype(jnp.float32) @ router_w.astype(jnp.float32).T
            probs = jax.nn.softmax(logits, axis=-1)
            rw, re = jax.lax.top_k(probs, TOP_K)
            if TOP_K > 1:
                rw = rw / jnp.maximum(rw.sum(-1, keepdims=True), 1e-12)
            rw = rw.astype(tokens.dtype)
            combine = jnp.zeros((N, E), tokens.dtype).at[jnp.arange(N)[:, None], re].set(rw)
            out = tokens
            for e in range(E):
                h = jax.nn.gelu(tokens @ w1[e] + b1[e], approximate=False)
                y = h @ w2[e] + b2[e]
                out = out + combine[:, e:e + 1] * y
            return out
        b, s, d = input_embeddings.shape
        tokens = input_embeddings.reshape(b * s, d)
        return _moe(tokens, router_w, w1, b1, w2, b2).reshape(b, s, d)
    edge_index = jnp.stack([src, dst])
    x = x + _L0_gnn_ref(_layernorm(x, axis=-1), edge_index, edge_weight, L0_gnn_W, L0_gnn_b, L0_gnn_W1, L0_gnn_b1, L0_gnn_W2, L0_gnn_b2)
    x = x + _L0_ffn_ref(_layernorm(x, axis=-1)[None], L0_ffn_router_w, L0_ffn_w1, L0_ffn_b1, L0_ffn_w2, L0_ffn_b2)[0]
    return x

_drawn_inputs = setup_inputs


def setup_inputs(seed=0):
    import zlib

    import numpy as np

    out = dict(_drawn_inputs(seed))
    spreads = {'L0_gnn_b': (0.0, 0.1),
     'L0_gnn_b1': (0.0, 0.1),
     'L0_gnn_b2': (0.0, 0.1),
     'L0_ffn_b1': (0.0, 0.33),
     'L0_ffn_b2': (0.0, 0.1)}
    factors = {}
    for name, (base, spread) in spreads.items():
        noise = np.random.default_rng([zlib.crc32(name.encode()), seed]).standard_normal(out[name].shape)
        drawn = base * np.exp(spread * noise) if base else spread * noise
        out[name] = jnp.asarray(drawn.astype(out[name].dtype))
    for name, factor in factors.items():
        out[name] = (out[name] * factor).astype(out[name].dtype)
    return out
```

```python
import concourse.bass as bass
from concourse import mybir
from contextlib import ExitStack

NODES, D, EDGES, EXPERTS = 6250, 256, 100000, 8
P = 128
KD = D // P
TILE = 125
TILES = NODES // TILE
PAIRS = TILES // 2
BLOCK = 8
COLS = -(-EDGES // (P * BLOCK)) * BLOCK
BLOCKS = COLS // BLOCK
FULL = EDGES // COLS
REST = EDGES - FULL * COLS
GROUP = 4
SHIFT = 9
RING = 8
GROUPS = -(-(COLS // GROUP + TILES) // RING) * RING
SLOT_TILES = GROUPS * GROUP
COUNT_COLS = 56
COUNT_STEPS = COLS // COUNT_COLS
EPS = 1e-5


def build(nc, x, src, dst, edge_weight, gnn_w, gnn_b, gnn_w1, gnn_b1, gnn_w2, gnn_b2,
          router_w, w1, b1, w2, b2, out):
    f32, bf16, i32, u32 = mybir.dt.float32, mybir.dt.bfloat16, mybir.dt.int32, mybir.dt.uint32
    ALU, ACT, AX = mybir.AluOpType, mybir.ActivationFunctionType, mybir.AxisListType
    ds = bass.ds
    assert GROUP * P == 1 << SHIFT and COLS % COUNT_COLS == 0 and BLOCKS % 2 == 0

    records = nc.dram_tensor("records", [P, SLOT_TILES * 3], f32, kind="Internal").ap()
    xw_table = nc.dram_tensor("xw_table", [NODES, D], f32, kind="Internal").ap()
    x_v = x.rearrange("(t p) d -> p t d", p=TILE)
    out_v = out.rearrange("(t p) d -> p t d", p=TILE)
    table_v = xw_table.rearrange("(t p) d -> p t d", p=TILE)
    record_rows = records.rearrange("p (t r) -> (p t) r", r=3)

    ctx = ExitStack()
    with ctx:
        def sb(name, shape, dt=f32):
            return ctx.enter_context(nc.sbuf_tensor(name, shape, dt))

        def sem(name):
            return ctx.enter_context(nc.semaphore(name))

        ident = sb("ident", [P, P])
        before = sb("before", [P, P], bf16)
        ones = sb("ones", [P, P], bf16)
        zeros = sb("zeros", [P, 2 * D], bf16)
        tile_ids = sb("tile_ids", [P, TILES])
        row_ids = sb("row_ids", [P, TILE])
        expert_ids = sb("expert_ids", [P, EXPERTS])
        rows = sb("rows", [P, RING * GROUP, D])
        spare = [rows[:, :, :].rearrange("p t d -> p (t d)"), 0]

        def early(n):
            spare[1] += n
            assert spare[1] <= RING * GROUP * D
            return spare[0][:, spare[1] - n:spare[1]]

        count_hot = early(COUNT_COLS * TILES).bitcast(bf16).rearrange("p (u c b) -> p u c b", u=2, b=TILES)
        hot_w = early(2 * BLOCK * TILES).rearrange("p (u c b) -> p u c b", u=2, b=TILES)
        row_hot = early(2 * BLOCK * TILE).rearrange("p (u c b) -> p u c b", u=2, b=TILE)
        ranks = early(BLOCK * TILES).rearrange("p (c b) -> p c b", b=TILES)
        picked = early(BLOCK * TILES).rearrange("p (c b) -> p c b", b=TILES)
        src_i = sb("src_i", [P, COLS], i32)
        dst_i = sb("dst_i", [P, COLS], i32)
        weight = sb("weight", [P, COLS])
        src_f = sb("src_f", [P, COLS])
        tile_f = sb("tile_f", [P, COLS])
        tile_i = src_i
        row_f = sb("row_f", [P, COLS])
        rec = sb("rec", [P, 2, BLOCK, 3])
        slot = sb("slot", [P, COLS], i32)
        hot = sb("hot", [P, 2, BLOCK + 1, TILES], bf16)
        slot_now = sb("slot_now", [P, 2, BLOCK], i32)
        index = sb("index", [P, RING, GROUP], i32)
        counts = sb("counts", [P, TILES])
        groups_i = sb("groups_i", [P, TILES], i32)
        groups_f = sb("groups_f", [P, TILES])
        cum = sb("cum", [P, TILES])
        first_f = sb("first_f", [P, TILES])
        end_i = sb("end_i", [P, TILES], i32)
        first_i = sb("first_i", [P, TILES], i32)
        total_i = sb("total_i", [P, 1], i32)
        start = sb("start", [P, TILES])
        pos_f = sb("pos_f", [P, BLOCK])
        pos_i = sb("pos_i", [P, BLOCK], i32)
        lane_i = sb("lane_i", [P, BLOCK], i32)
        at_i = sb("at_i", [P, BLOCK], i32)
        deg = sb("deg", [TILE, TILES])
        positive = sb("positive", [TILE, TILES])
        dinv = sb("dinv", [TILE, TILES])
        w_sb = sb("w_sb", [P, KD, D])
        w1_sb = sb("w1_sb", [P, KD, D])
        w2_sb = sb("w2_sb", [P, KD, D])
        router_sb = sb("router_sb", [P, KD, EXPERTS])
        ew1 = sb("ew1", [P, EXPERTS, KD, D])
        ew2 = sb("ew2", [P, EXPERTS, KD, D])
        eb1 = sb("eb1", [P, EXPERTS, KD])
        eb2 = sb("eb2", [EXPERTS, D])
        b_bc = sb("b_bc", [TILE, D])
        b1_col = sb("b1_col", [P, KD])
        b2_bc = sb("b2_bc", [TILE, D])
        x_in = sb("x_in", [TILE, 2, D])
        xn = sb("xn", [TILE, 2, D])
        xn_t = sb("xn_t", [P, KD, 2 * TILE])
        xw = sb("xw", [TILE, TILES, D])
        meta = sb("meta", [P, SLOT_TILES, 3])
        select = sb("select", [P, GROUP, TILE])
        h7 = sb("h7", [TILE, 2, D])
        h7_t = sb("h7_t", [P, KD, 2 * TILE])
        r1_t = sb("r1_t", [P, KD, 2 * TILE])
        x1 = sb("x1", [TILE, 2, D])
        stats_all = sb("stats_all", [TILE, TILES, 6])
        moments_all = sb("moments_all", [TILE, TILES, 2])
        rstd_all = sb("rstd_all", [TILE, TILES])
        stats = sb("stats", [TILE, 2, 6])
        moments = sb("moments", [TILE, 2, 2])
        rstd = sb("rstd", [TILE, 2])
        var = sb("var", [TILE, 2])
        root_t = sb("root_t", [TILE, TILES])
        tok = sb("tok", [TILE, 2, D])
        tok_new = sb("tok_new", [P, KD, 2 * TILE])
        tok_t = sb("tok_t", [P, KD, 2 * TILE])
        top = sb("top", [TILE, 2])
        shifted = sb("shifted", [TILE, 2, EXPERTS])
        expo = sb("expo", [TILE, 2, EXPERTS])
        esum = sb("esum", [TILE, 2])
        probs = sb("probs", [TILE, 2, EXPERTS])
        best = sb("best", [TILE, 2, 8])
        best_at = sb("best_at", [TILE, 2, 8], u32)
        best_f = sb("best_f", [TILE, 2, 8])
        two = sb("two", [TILE, 2])
        share = sb("share", [TILE, 2, 2])
        second = sb("second", [TILE, 2, EXPERTS])
        comb_new = sb("comb_new", [TILE, 2, EXPERTS])
        comb = sb("comb", [TILE, 2, EXPERTS])
        comb_t = sb("comb_t", [EXPERTS, 2 * TILE])
        hid = sb("hid", [P, 2, KD, 2 * TILE])
        acc = sb("acc", [TILE, 2, D])
        acc_first = sb("acc_first", [TILE, 2, D])
        out_sb = sb("out_sb", [TILE, 2, D])

        def bank(name):
            return ctx.enter_context(nc.psum_tensor(name, [P, 512], f32))
        ps_sum, ps_tp, ps_m1, ps_o2 = bank("ps_sum"), bank("ps_tp"), bank("ps_m1"), bank("ps_o2")
        ps_g = [bank("ps_g0"), bank("ps_g1")]
        ps_y = [bank("ps_y0"), bank("ps_y1")]
        ps_count = ps_sum[:, 0:BLOCK * TILES]
        ps_rank = [ps_g[u][:, 0:(BLOCK + 1) * TILES].rearrange("p (c b) -> p c b", b=TILES) for u in range(2)]
        ps_deg = ps_y[0][0:TILE, 0:TILES]

        def halves(ps):
            return ps[:, 0:KD * 2 * TILE].rearrange("p (k n) -> p k n", k=KD)

        def nodes(ps):
            return ps[0:TILE, :].rearrange("p (s d) -> p s d", s=2)

        s_const = sem("s_const")
        s_pad = sem("s_pad")
        s_zero = sem("s_zero")
        s_fill = sem("s_fill")
        s_src, s_dst, s_wt = sem("s_src"), sem("s_dst"), sem("s_wt")
        s_weights = sem("s_weights")
        s_chain = sem("s_chain")
        s_settle, s_settle_pool = sem("s_settle"), sem("s_settle_pool")
        s_hotc = sem("s_hotc")
        s_counted = sem("s_counted")
        s_base = sem("s_base")
        s_hot = sem("s_hot")
        s_ranked = sem("s_ranked")
        s_degd = sem("s_degd")
        s_rchain = sem("s_rchain")
        s_slot = sem("s_slot")
        s_row = sem("s_row")
        s_now = sem("s_now")
        s_index = sem("s_index")
        s_scat = [sem(f"s_scat{u}") for u in range(2)]
        s_xin = sem("s_xin")
        s_stats = sem("s_stats")
        s_xn = sem("s_xn")
        s_xnt = sem("s_xnt")
        s_xnts = sem("s_xnts")
        s_xwp = sem("s_xwp")
        s_xw = sem("s_xw")
        s_table = sem("s_table")
        s_meta = sem("s_meta")
        s_rows = [sem(f"s_rows{u}") for u in range(GROUP)]
        s_sel = sem("s_sel")
        s_used = sem("s_used")
        s_sum = sem("s_sum")
        s_h7 = sem("s_h7")
        s_h7t, s_h7ts = sem("s_h7t"), sem("s_h7ts")
        s_m1, s_r1 = sem("s_m1"), sem("s_r1")
        s_o2, s_x1 = sem("s_o2"), sem("s_x1")
        s_xp = sem("s_xp")
        s_achain = sem("s_achain")
        s_bchain = sem("s_bchain")
        s_tok, s_tokt, s_tokn, s_tokc = sem("s_tok"), sem("s_tokt"), sem("s_tokn"), sem("s_tokc")
        s_log, s_shift, s_exp = sem("s_log"), sem("s_shift"), sem("s_exp")
        s_comb, s_ct, s_cts, s_by, s_acc = sem("s_comb"), sem("s_ct"), sem("s_cts"), sem("s_by"), sem("s_acc")
        s_g, s_gelu = sem("s_g"), sem("s_gelu")
        s_y = sem("s_y")
        s_yused = sem("s_yused")
        s_out, s_store = sem("s_out"), sem("s_store")

        WEIGHT_LOADS = 12
        block = ctx.enter_context(nc.Block())

        @block.sync
        def _(sp):
            sp.wait_ge(s_pad, 3)
            lots = [(0, FULL // 16 * 16, COLS), (FULL // 16 * 16, FULL, COLS), (FULL, FULL + 1, REST)]
            for arr, tile, s in ((src, src_i, s_src), (edge_weight, weight, s_wt), (dst, dst_i, s_dst)):
                for lo, hi, n in lots:
                    sp.dma_start(tile[lo:hi, 0:n],
                                 arr[lo * COLS:(hi - 1) * COLS + n].rearrange("(p c) -> p c", c=n)).then_inc(s, 16)
            sp.wait_ge(s_zero, 1)
            sp.dma_start(records, meta[:, :, :].rearrange("p t r -> p (t r)")).then_inc(s_fill, 16)

            sp.dma_start(xw[:, :, :], x_v).then_inc(s_xin, 16)

            def load_x(pair):
                sp.dma_start(x_in[:, :, :], x_v[:, ds(pair * 2, 2), :]).then_inc(s_xp, 16)

            sp.dma_start(w_sb[:, :, :], gnn_w.rearrange("(k p) d -> p k d", p=P)).then_inc(s_weights, 16)
            sp.dma_start(w1_sb[:, :, :], gnn_w1.rearrange("(k p) d -> p k d", p=P)).then_inc(s_weights, 16)
            sp.dma_start(w2_sb[:, :, :], gnn_w2.rearrange("(k p) d -> p k d", p=P)).then_inc(s_weights, 16)
            for k in range(KD):
                sp.dma_start(router_sb[:, k, :], router_w[:, k * P:(k + 1) * P].rearrange("e p -> p e"),
                             allow_slow_non_contiguous=True).then_inc(s_weights, 16)
            sp.dma_start(ew1[:, :, :, :], w1.rearrange("e (k p) d -> p e k d", p=P)).then_inc(s_weights, 16)
            sp.dma_start(ew2[:, :, :, :], w2.rearrange("e (k p) d -> p e k d", p=P)).then_inc(s_weights, 16)
            sp.dma_start(eb2[:, :], b2).then_inc(s_weights, 16)
            sp.dma_start(b_bc[:, :], gnn_b.partition_broadcast(TILE)).then_inc(s_weights, 16)
            sp.dma_start(b2_bc[:, :], gnn_b2.partition_broadcast(TILE)).then_inc(s_weights, 16)
            with nc.allow_non_contiguous_dma(reason="bias columns"):
                sp.dma_start(b1_col[:, :], gnn_b1.rearrange("(k p) -> p k", p=P)).then_inc(s_weights, 16)
                sp.dma_start(eb1[:, :, :], b1.rearrange("e (k p) -> p e k", p=P)).then_inc(s_weights, 16)

            load_x(0)
            with sp.Fori(0, PAIRS) as i:
                sp.wait_ge(s_xw, i * 2 + 2)
                sp.dma_start(table_v[:, ds(i * 2, 2), :], xw[:, ds(i * 2, 2), :]).then_inc(s_table, 16)

            for u in range(2):
                sp.wait_ge(s_scat[u], 16 * COLS // 2)
            sp.dma_start(meta[:, :, :].rearrange("p t r -> p (t r)"), records).then_inc(s_meta, 16)

            def store(pair):
                sp.dma_start(out_v[:, ds(pair * 2, 2), :], out_sb[:, :, :]).then_inc(s_store, 16)

            with sp.Fori(1, PAIRS) as q:
                sp.wait_ge(s_x1, q)
                load_x(q)
                sp.wait_ge(s_out, q)
                store(q - 1)
            sp.wait_ge(s_out, PAIRS)
            store(PAIRS - 1)
            sp.wait_ge(s_store, 16 * PAIRS)

        @block.gpsimd
        def _(pool):
            pool.memset(meta[:, :, :], 0.0).then_inc(s_zero, 1)
            pool.iota(tile_ids[:, :], [[1, TILES]], base=0, channel_multiplier=0,
                      allow_small_or_imprecise_dtypes=True).then_inc(s_const, 1)
            pool.iota(row_ids[:, :], [[1, TILE]], base=0, channel_multiplier=0,
                      allow_small_or_imprecise_dtypes=True).then_inc(s_const, 1)
            pool.iota(expert_ids[:, :], [[1, EXPERTS]], base=0, channel_multiplier=0,
                      allow_small_or_imprecise_dtypes=True).then_inc(s_const, 1)
            pool.memset(ident[:, :], 0.0).then_inc(s_const, 1)
            pool.memset(before[:, :], 1.0).then_inc(s_const, 1)
            pool.memset(ones[:, :], 1.0).then_inc(s_const, 1)
            pool.memset(zeros[:, :], 0.0).then_inc(s_const, 1)
            pool.memset(hot[:, :, :, :], 0.0).then_inc(s_const, 1)
            pool.wait_ge(s_const, 8)
            pool.affine_select(out=ident[:, :], in_=ident[:, :], compare_op=ALU.not_equal, fill=1.0,
                               base=0, pattern=[[-1, P]], channel_multiplier=1).then_inc(s_const, 1)
            pool.affine_select(out=before[:, :], in_=before[:, :], compare_op=ALU.is_gt, fill=0.0,
                               base=0, pattern=[[1, P]], channel_multiplier=-1).then_inc(s_const, 1)
            pool.wait_ge(s_fill, 16)
            with pool.Fori(0, BLOCKS // 2) as i:
                for u in range(2):
                    k = i * 2 + u
                    pool.wait_ge(s_now, k * 4 + 4)
                    pool.sem_inc(s_settle_pool, 1)
                    for c in range(BLOCK):
                        pool.indirect_dma_start(
                            out=record_rows,
                            in_=rec[:, u, c, :],
                            out_offset=bass.IndirectOffsetOnAxis(ap=slot_now[:, u, c:c + 1], axis=0),
                            in_offset=None).then_inc(s_scat[u], 16)
            pool.wait_ge(s_base, 1)
            total = pool.value_load(total_i[0:1, 0:1], min_val=1, max_val=GROUPS // RING)
            pool.wait_ge(s_meta, 16)
            pool.wait_ge(s_table, 16 * PAIRS)
            with pool.Fori(0, total) as i:
                for v in range(RING):
                    k = i * RING + v
                    pool.wait_ge(s_used, k * GROUP + GROUP)
                    pool.tensor_copy(index[:, v, :], meta[:, ds(k * GROUP, GROUP), 0].bitcast(i32)).then_inc(s_index, 1)
                    pool.wait_ge(s_index, k + 1)
                    for u in range(GROUP):
                        pool.wait_ge(s_rows[u], k * 16)
                        pool.sem_inc(s_settle_pool, 1)
                        pool.indirect_dma_start(
                            out=rows[:, v * GROUP + u, :], out_offset=None, in_=xw_table,
                            in_offset=bass.IndirectOffsetOnAxis(ap=index[:, v, u:u + 1], axis=0)).then_inc(s_rows[u], 16)

        @block.vector
        def _(dve):
            class Chain:
                def __init__(self, s, base=0):
                    self.s, self.base, self.n = s, base, 0

                def settle(self):
                    dve.sem_inc(s_settle, 1)

                def link(self, ins):
                    self.n += 1
                    ins.then_inc(self.s, 1)
                    dve.wait_ge(self.s, self.base + self.n)

            V = nc.vector
            ch = Chain(s_chain)
            lo_p = FULL // 32 * 32
            V.memset(src_i[lo_p:P, REST:COLS], NODES - 1).then_inc(s_pad, 1)
            V.memset(dst_i[lo_p:P, REST:COLS], 0).then_inc(s_pad, 1)
            V.memset(weight[lo_p:P, REST:COLS], 0.0).then_inc(s_pad, 1)

            dve.wait_ge(s_src, 48)
            ch.link(V.tensor_copy(src_f[:, :], src_i[:, :]))
            ch.link(V.tensor_scalar(tile_i[:, :], src_f[:, :], 1.0 / TILE, 0.001, ALU.mult, ALU.add))
            ch.link(V.tensor_copy(tile_f[:, :], tile_i[:, :]))
            ch.link(V.scalar_tensor_tensor(out=row_f[:, :], in0=tile_f[:, :], scalar=-float(TILE), in1=src_f[:, :],
                                           op0=ALU.mult, op1=ALU.add))
            ch.link(V.tensor_scalar(src_f[:, :], row_f[:, :], 0.0, None, ALU.is_lt))
            ch.link(V.tensor_tensor(tile_f[:, :], tile_f[:, :], src_f[:, :], ALU.subtract))
            ch.link(V.scalar_tensor_tensor(out=row_f[:, :], in0=src_f[:, :], scalar=float(TILE), in1=row_f[:, :],
                                           op0=ALU.mult, op1=ALU.add))
            dve.sem_inc(s_row, 1)

            dve.wait_ge(s_const, 10)
            with dve.Fori(0, COUNT_STEPS // 2) as i:
                for u in range(2):
                    dve.wait_ge(s_counted, i * 2 + u + 1)
                    V.tensor_tensor(
                        count_hot[:, u, :, :],
                        tile_f[:, ds(i * (2 * COUNT_COLS) + u * COUNT_COLS, COUNT_COLS)].unsqueeze(2).to_broadcast([P, COUNT_COLS, TILES]),
                        tile_ids[:, :].unsqueeze(1).to_broadcast([P, COUNT_COLS, TILES]), ALU.is_equal).then_inc(s_hotc, 1)
            dve.wait_ge(s_counted, COUNT_STEPS + 3)
            ch.link(V.tensor_reduce(counts[:, :], ps_count.rearrange("p (c b) -> p b c", b=TILES), AX.X, ALU.add))
            ch.link(V.tensor_scalar(groups_i[:, :], counts[:, :], float((1 << SHIFT) - 1), None, ALU.add))
            ch.link(V.tensor_scalar(groups_i[:, :], groups_i[:, :], SHIFT, None, ALU.arith_shift_right))
            ch.link(V.tensor_scalar(groups_i[:, :], groups_i[:, :], 1, None, ALU.max))
            ch.link(V.tensor_copy(groups_f[:, :], groups_i[:, :]))
            ch.link(V.memset(start[:, :], 1.0))
            ch.link(V.tensor_tensor_scan(cum[:, :], start[:, :], groups_f[:, :], 0.0, ALU.mult, ALU.add))
            ch.link(V.tensor_tensor(first_f[:, :], cum[:, :], groups_f[:, :], ALU.subtract))
            ch.link(V.tensor_scalar(total_i[:, :], cum[:, TILES - 1:TILES], float(RING - 1), None, ALU.add))
            ch.link(V.tensor_scalar(total_i[:, :], total_i[:, :], RING.bit_length() - 1, None, ALU.arith_shift_right))
            ch.link(V.tensor_copy(end_i[:, :], cum[:, :]))
            ch.link(V.tensor_copy(first_i[:, :], first_f[:, :]))
            dve.sem_inc(s_base, 1)
            ch.link(V.tensor_scalar(start[:, :], first_f[:, :], float(1 << SHIFT), None, ALU.mult))

            dve.wait_ge(s_wt, 48)
            PER_BLOCK = 7

            def one_hots(u, cols):
                V.tensor_tensor(hot[:, u, 0:BLOCK, :], tile_f[:, cols].unsqueeze(2).to_broadcast([P, BLOCK, TILES]),
                                tile_ids[:, :].unsqueeze(1).to_broadcast([P, BLOCK, TILES]), ALU.is_equal).then_inc(s_hot, 1)
                V.tensor_tensor(row_hot[:, u, :, :], row_f[:, cols].unsqueeze(2).to_broadcast([P, BLOCK, TILE]),
                                row_ids[:, :].unsqueeze(1).to_broadcast([P, BLOCK, TILE]), ALU.is_equal).then_inc(s_hot, 1)

            def weigh(k, u, cols):
                dve.wait_ge(s_hot, k * 3 + 2)
                V.tensor_tensor(hot_w[:, u, :, :], hot[:, u, 0:BLOCK, :],
                                weight[:, cols].unsqueeze(2).to_broadcast([P, BLOCK, TILES]), ALU.mult).then_inc(s_hot, 1)

            def slots(k, u, cols):
                rc = Chain(s_rchain, k * PER_BLOCK)
                dve.wait_ge(s_ranked, k + 1)
                rc.link(V.tensor_tensor(ranks[:, :, :], ps_rank[u][:, 0:BLOCK, :],
                                        start[:, :].unsqueeze(1).to_broadcast([P, BLOCK, TILES]), ALU.add))
                rc.link(V.tensor_tensor(start[:, :], start[:, :], ps_rank[u][:, BLOCK, :], ALU.add))
                rc.link(V.tensor_tensor(picked[:, :, :], ranks[:, :, :], hot[:, u, 0:BLOCK, :], ALU.mult))
                rc.link(V.tensor_reduce(pos_f[:, :], picked[:, :, :], AX.X, ALU.add))
                rc.link(V.tensor_copy(pos_i[:, :], pos_f[:, :]))
                rc.link(V.tensor_scalar(lane_i[:, :], pos_i[:, :], P - 1, None, ALU.bitwise_and))
                rc.link(V.tensor_scalar(at_i[:, :], pos_i[:, :], 7, None, ALU.arith_shift_right))
                V.scalar_tensor_tensor(out=slot[:, cols], in0=lane_i[:, :], scalar=float(SLOT_TILES), in1=at_i[:, :],
                                       op0=ALU.mult, op1=ALU.add).then_inc(s_slot, 1)
                assert rc.n == PER_BLOCK

            def block_cols(i, u):
                return ds(i * (2 * BLOCK) + u * BLOCK, BLOCK)

            def turn(i, u):
                k = i * 2 + u
                dve.wait_ge(s_degd, k + 2)
                one_hots(1 - u, block_cols(i, u + 1))
                weigh(k + 1, 1 - u, block_cols(i, u + 1))
                slots(k, u, block_cols(i, u))

            one_hots(0, block_cols(0, 0))
            weigh(0, 0, block_cols(0, 0))
            dve.wait_ge(s_xin, 16)
            with dve.Fori(0, BLOCKS // 2 - 1) as i:
                turn(i, 0)
                turn(i, 1)
            turn(BLOCKS // 2 - 1, 0)
            slots(BLOCKS - 1, 1, block_cols(BLOCKS // 2 - 1, 1))

            def inverse_root(chain, y, v, t):
                chain.link(V.tensor_scalar(t.bitcast(i32), v.bitcast(i32), 1, None, ALU.arith_shift_right))
                chain.link(V.tensor_scalar(y.bitcast(i32), t.bitcast(i32), -1.0, float(0x5f3759df), ALU.mult, ALU.add))
                for _ in range(3):
                    chain.link(V.scalar_tensor_tensor(out=t, in0=y, scalar=-0.5, in1=v, op0=ALU.mult, op1=ALU.mult))
                    chain.link(V.tensor_tensor(t, t, y, ALU.mult))
                    chain.link(V.scalar_tensor_tensor(out=y, in0=t, scalar=1.5, in1=y, op0=ALU.add, op1=ALU.mult))

            dve.wait_ge(s_degd, BLOCKS + 3)
            ch.link(V.tensor_scalar(deg[:, :], ps_deg, 1.0, None, ALU.add))
            ch.link(V.tensor_scalar(positive[:, :], deg[:, :], 0.0, None, ALU.is_gt))
            ch.link(V.tensor_scalar(deg[:, :], deg[:, :], 1e-30, None, ALU.max))
            inverse_root(ch, dinv[:, :], deg[:, :], root_t[:, :])
            ch.link(V.tensor_tensor(dinv[:, :], dinv[:, :], positive[:, :], ALU.mult))

            def layer_norm(chain, of, to, last):
                for s in range(2):
                    chain.link(V.bn_stats(stats[:, s, :], of[:, s, :]))
                chain.settle()
                for s in range(2):
                    if s:
                        chain.settle()
                    chain.link(V.bn_aggr(moments[:, s, :], stats[:, s, :]))
                chain.link(V.tensor_scalar(var[:, :], moments[:, :, 1], EPS, None, ALU.add))
                inverse_root(chain, rstd[:, :], var[:, :], root_t[:, 0:2])
                for s in range(2):
                    last(V.tensor_scalar(to[:, s, :], of[:, s, :], moments[:, s, 0:1], rstd[:, s:s + 1],
                                         ALU.subtract, ALU.mult))

            with dve.Fori(0, PAIRS) as i:
                for s in range(2):
                    V.bn_stats(stats_all[:, ds(i * 2 + s, 1), :].rearrange("p t c -> p (t c)"),
                               xw[:, ds(i * 2 + s, 1), :].rearrange("p t d -> p (t d)")).then_inc(s_stats, 1)
            dve.wait_ge(s_stats, TILES)
            ch.settle()
            for t in range(TILES):
                V.bn_aggr(moments_all[:, t, :], stats_all[:, t, :]).then_inc(s_stats, 1)
            dve.wait_ge(s_stats, 2 * TILES)
            ch.link(V.tensor_scalar(deg[:, :], moments_all[:, :, 1], EPS, None, ALU.add))
            inverse_root(ch, rstd_all[:, :], deg[:, :], root_t[:, :])

            with dve.Fori(0, PAIRS) as i:
                dve.wait_ge(s_xnt, i)
                for s in range(2):
                    V.tensor_scalar(xn[:, s, :], xw[:, ds(i * 2 + s, 1), :].rearrange("p t d -> p (t d)"),
                                    moments_all[:, ds(i * 2 + s, 1), 0:1].rearrange("p t c -> p (t c)"),
                                    rstd_all[:, ds(i * 2 + s, 1)], ALU.subtract, ALU.mult).then_inc(s_xn, 1)
                dve.wait_ge(s_xnt, i + 1)
                V.tensor_copy(xn_t[:, :, :], halves(ps_tp)).then_inc(s_xnts, 1)
                dve.wait_ge(s_xwp, i + 1)
                for s in range(2):
                    V.tensor_scalar(xw[:, ds(i * 2 + s, 1), :].rearrange("p t d -> p (t d)"), nodes(ps_o2)[:, s, :],
                                    dinv[:, ds(i * 2 + s, 1)], None, ALU.mult).then_inc(s_xw, 1)

            dve.wait_ge(s_meta, 16)
            dve.sem_inc(s_yused, 1)

            def selectors(begin, end):
                with dve.Fori(begin, end) as k:
                    for u in range(GROUP):
                        if u % 2 == 0:
                            dve.wait_ge(s_used, k * GROUP + u + 2 + (RING - 1) * GROUP)
                        V.tensor_scalar(select[:, u, :], row_ids[:, :],
                                        meta[:, ds(k * GROUP + u, 1), 1:2].rearrange("p t r -> p (t r)"),
                                        meta[:, ds(k * GROUP + u, 1), 2:3].rearrange("p t r -> p (t r)"),
                                        ALU.is_equal, ALU.mult).then_inc(s_sel, 1)

            selectors(0, 1)

            def both(v, n):
                return v.unsqueeze(2).to_broadcast([TILE, 2, n])

            def body(pair, first, last):
                prev = pair - 1
                A = Chain(s_achain, pair * A_LINKS)

                def add_expert(e):
                    if first:
                        return
                    dve.wait_ge(s_y, prev * EXPERTS + e + 2)
                    if e == EXPERTS - 1:
                        dve.wait_ge(s_store, prev * 16)
                    for s in range(2):
                        ins = V.scalar_tensor_tensor(
                            out=(out_sb if e == EXPERTS - 1 else acc)[:, s, :], in0=nodes(ps_y[e % 2])[:, s, :],
                            scalar=comb[:, s, e:e + 1], in1=(acc if e else acc_first)[:, s, :], op0=ALU.mult, op1=ALU.add)
                        ins.then_inc(s_bchain, 1)
                    dve.wait_ge(s_bchain, prev * 2 * EXPERTS + 2 * e + 2)
                    dve.sem_inc(s_yused, 1)

                if not last:
                    begin = dve.value_load(first_i[0:1, ds(pair * 2, 1)], min_val=0, max_val=GROUPS - 3)
                    end = dve.value_load(end_i[0:1, ds(pair * 2 + 1, 1)], min_val=2, max_val=GROUPS - 2)
                    selectors(begin + 1, end + 1)
                    dve.wait_ge(s_sum, pair * 2 + 2)
                    for s in range(2):
                        V.scalar_tensor_tensor(out=h7[:, s, :], in0=nodes(ps_sum)[:, s, :], scalar=dinv[:, ds(pair * 2 + s, 1)],
                                               in1=b_bc[:, :], op0=ALU.mult, op1=ALU.add).then_inc(s_h7, 1)
                add_expert(0)
                add_expert(1)
                if not last:
                    dve.wait_ge(s_o2, pair + 1)
                    dve.wait_ge(s_xp, pair * 16 + 16)
                    A.link(V.tensor_tensor(x1[:, :, :], nodes(ps_o2), x_in[:, :, :], ALU.add))
                    dve.sem_inc(s_x1, 1)
                    A.link(V.tensor_tensor(x1[:, :, :], x1[:, :, :], b2_bc[:, :].unsqueeze(1).to_broadcast([TILE, 2, D]), ALU.add))
                    layer_norm(A, x1, tok, lambda ins: ins.then_inc(s_tok, 1))
                add_expert(2)
                add_expert(3)
                if not last:
                    logits = ps_o2[0:TILE, 0:2 * EXPERTS].rearrange("p (s e) -> p s e", e=EXPERTS)
                    dve.wait_ge(s_log, pair + 1)
                    A.link(V.tensor_reduce(top[:, :], logits, AX.X, ALU.max))
                    V.tensor_tensor(shifted[:, :, :], logits, both(top[:, :], EXPERTS), ALU.subtract).then_inc(s_shift, 1)
                add_expert(4)
                if not last:
                    dve.wait_ge(s_exp, pair + 1)
                    A.link(V.tensor_reduce(esum[:, :], expo[:, :, :], AX.X, ALU.add))
                    A.link(V.reciprocal(esum[:, :], esum[:, :]))
                    A.link(V.tensor_tensor(probs[:, :, :], expo[:, :, :], both(esum[:, :], EXPERTS), ALU.mult))
                    for s in range(2):
                        A.settle()
                        A.link(V.max(best[:, s, :], probs[:, s, :]))
                    for s in range(2):
                        A.settle()
                        A.link(V.max_index(best_at[:, s, :], best[:, s, :], probs[:, s, :]))
                    A.link(V.tensor_copy(best_f[:, :, :], best_at[:, :, :]))
                    A.link(V.tensor_tensor(two[:, :], best[:, :, 0], best[:, :, 1], ALU.add))
                    A.link(V.tensor_scalar(two[:, :], two[:, :], 1e-12, None, ALU.max))
                    A.link(V.reciprocal(two[:, :], two[:, :]))
                    A.link(V.tensor_tensor(share[:, :, :], best[:, :, 0:2], both(two[:, :], 2), ALU.mult))
                    for s in range(2):
                        A.link(V.tensor_scalar(second[:, s, :], expert_ids[0:TILE, :], best_f[:, s, 1:2], share[:, s, 1:2],
                                               ALU.is_equal, ALU.mult))
                    for s in range(2):
                        A.link(V.tensor_scalar(comb_new[:, s, :], expert_ids[0:TILE, :], best_f[:, s, 0:1], share[:, s, 0:1],
                                               ALU.is_equal, ALU.mult))
                    A.link(V.tensor_tensor(comb_new[:, :, :], comb_new[:, :, :], second[:, :, :], ALU.add))
                    dve.sem_inc(s_comb, 1)
                add_expert(5)
                if not last:
                    dve.wait_ge(s_tok, pair * 2 + 2)
                    A.link(V.tensor_tensor(acc_first[:, :, :], x1[:, :, :], tok[:, :, :], ALU.add))
                add_expert(6)
                if not last:
                    dve.wait_ge(s_by, pair + 1)
                    A.link(V.tensor_tensor(acc_first[:, :, :], nodes(ps_o2), acc_first[:, :, :], ALU.add))
                    dve.sem_inc(s_acc, 1)
                add_expert(7)
                if not first:
                    dve.sem_inc(s_out, 1)
                if not last:
                    A.link(V.tensor_copy(comb[:, :, :], comb_new[:, :, :]))
                    assert A.n == A_LINKS, A.n

            A_LINKS = 39
            body(0, True, False)
            with dve.Fori(1, PAIRS) as pair:
                body(pair, False, False)
            body(PAIRS, False, True)

        @block.tensor
        def _(pe):
            T = nc.tensor
            pe.wait_ge(s_const, 10)
            T.matmul(ps_count, ones[:, :], zeros[:, 0:BLOCK * TILES], start=True, stop=False).then_inc(s_counted, 2)
            with pe.Fori(0, COUNT_STEPS // 2) as i:
                for u in range(2):
                    pe.wait_ge(s_hotc, i * 2 + u + 1)
                    for c in range(0, COUNT_COLS, BLOCK):
                        last = T.matmul(ps_count, ones[:, :], count_hot[:, u, c:c + BLOCK, :].rearrange("p c b -> p (c b)"), start=False, stop=False)
                    last.then_inc(s_counted, 1)
            T.matmul(ps_count, ones[:, :], zeros[:, 0:BLOCK * TILES], start=False, stop=True).then_inc(s_counted, 1)

            T.matmul(ps_deg, zeros[:, 0:TILE], zeros[:, 0:TILES], start=True, stop=False).then_inc(s_degd, 2)
            with pe.Fori(0, BLOCKS // 2) as i:
                for u in range(2):
                    k = i * 2 + u
                    pe.wait_ge(s_hot, k * 3 + 1)
                    T.matmul(ps_rank[u], before[:, :], hot[:, u, :, :], start=True, stop=False)
                    for c in range(BLOCK):
                        last = T.matmul(ps_rank[u][:, c + 1:BLOCK + 1, :], ones[:, :],
                                        hot[:, u, c:c + 1, :].to_broadcast([P, BLOCK - c, TILES]), start=False, stop=c == BLOCK - 1)
                    last.then_inc(s_ranked, 1)
                    pe.wait_ge(s_hot, k * 3 + 3)
                    for c in range(BLOCK):
                        last = T.matmul(ps_deg, row_hot[:, u, c, :], hot_w[:, u, c, :], start=False, stop=False)
                    last.then_inc(s_degd, 1)
            T.matmul(ps_deg, zeros[:, 0:TILE], zeros[:, 0:TILES], start=False, stop=True).then_inc(s_degd, 1)

            def transposes(of, s_of, base, per_tile=True):
                for s in range(2):
                    pe.wait_ge(s_of, base + s + 1)
                    for kd in range(KD):
                        last = T.transpose(halves(ps_tp)[:, kd, s * TILE:(s + 1) * TILE], of[:, s, kd * P:(kd + 1) * P],
                                           ident[0:TILE, 0:TILE])
                return last

            def by_nodes(ps, lhs, rhs):
                for s in range(2):
                    for kd in range(KD):
                        last = T.matmul(nodes(ps)[:, s, :], lhs[:, kd, s * TILE:(s + 1) * TILE], rhs[:, kd, :],
                                        start=kd == 0, stop=kd == KD - 1)
                return last

            def by_features(ps, lhs, rhs):
                for f in range(KD):
                    for kd in range(KD):
                        last = T.matmul(halves(ps)[:, f, :], lhs[:, kd, f * P:(f + 1) * P], rhs[:, kd, :],
                                        start=kd == 0, stop=kd == KD - 1)
                return last

            pe.wait_ge(s_weights, 16 * WEIGHT_LOADS)
            with pe.Fori(0, PAIRS) as i:
                pe.wait_ge(s_xnts, i)
                transposes(xn, s_xn, i * 2).then_inc(s_xnt, 1)
                pe.wait_ge(s_xnts, i + 1)
                pe.wait_ge(s_xw, i * 2)
                by_nodes(ps_o2, xn_t, w_sb).then_inc(s_xwp, 1)

            pe.wait_ge(s_xw, PAIRS * 2)
            pe.wait_ge(s_base, 1)
            pe.sem_inc(s_used, RING * GROUP)
            pe.sem_inc(s_y, 1)

            def tile_sum(pair, s, begin, end):
                tile = pair * 2 + s
                total = nodes(ps_sum)[:, s, :]
                T.matmul(total, zeros[0:P, 0:TILE], zeros[:, 0:D], start=True, stop=False)
                with pe.Fori(begin, end) as k:
                    ring = (k % RING) * GROUP
                    for u in range(GROUP):
                        pe.wait_ge(s_rows[u], k * 16 + 16)
                        pe.wait_ge(s_sel, k * GROUP + u + 1)
                        T.matmul(total, select[:, u, :], rows[:, ds(ring + u, 1), :].rearrange("p c d -> p (c d)"),
                                 start=False, stop=False).then_inc(s_used, 1)
                T.matmul(total, ident[0:TILE, 0:TILE], xw[:, ds(tile, 1), :].rearrange("p c d -> p (c d)"),
                         start=False, stop=True).then_inc(s_sum, 1)

            def body(pair, first, last):
                prev = pair - 1

                def up(e):
                    if first:
                        return
                    if e == 0:
                        pe.wait_ge(s_tokc, prev + 1)
                    by_features(ps_g[e % 2], ew1[:, e, :, :], tok_t).then_inc(s_g, 1)

                def down(e):
                    if first:
                        return
                    pe.wait_ge(s_gelu, prev * 2 * EXPERTS + 2 * e + 2)
                    pe.wait_ge(s_yused, prev * EXPERTS + e)
                    by_nodes(ps_y[e % 2], hid[:, e % 2, :, :], ew2[:, e, :, :]).then_inc(s_y, 1)

                if not last:
                    pe.wait_ge(s_h7, pair * 2)
                    begin = pe.value_load(first_i[0:1, ds(pair * 2, 1)], min_val=0, max_val=GROUPS - 2)
                    middle = pe.value_load(end_i[0:1, ds(pair * 2, 1)], min_val=1, max_val=GROUPS - 1)
                    end = pe.value_load(end_i[0:1, ds(pair * 2 + 1, 1)], min_val=2, max_val=GROUPS)
                    tile_sum(pair, 0, begin, middle)
                    tile_sum(pair, 1, middle, end)
                up(0)
                up(1)
                if not last:
                    pe.wait_ge(s_tokc, pair)
                    transposes(h7, s_h7, pair * 2).then_inc(s_h7t, 1)
                down(0)
                if not last:
                    pe.wait_ge(s_h7ts, pair + 1)
                    pe.wait_ge(s_cts, pair)
                    by_features(ps_m1, w1_sb, h7_t).then_inc(s_m1, 1)
                up(2)
                down(1)
                if not last:
                    pe.wait_ge(s_r1, pair * 2 + 2)
                    pe.wait_ge(s_acc, pair)
                    by_nodes(ps_o2, r1_t, w2_sb).then_inc(s_o2, 1)
                up(3)
                down(2)
                up(4)
                down(3)
                if not last:
                    transposes(tok, s_tok, pair * 2).then_inc(s_tokt, 1)
                up(5)
                if not last:
                    pe.wait_ge(s_tokn, pair + 1)
                    pe.wait_ge(s_x1, pair + 1)
                    for s in range(2):
                        for kd in range(KD):
                            done = T.matmul(ps_o2[0:TILE, s * EXPERTS:(s + 1) * EXPERTS],
                                            tok_new[:, kd, s * TILE:(s + 1) * TILE], router_sb[:, kd, :],
                                            start=kd == 0, stop=kd == KD - 1)
                    done.then_inc(s_log, 1)
                down(4)
                up(6)
                down(5)
                up(7)
                if not last:
                    pe.wait_ge(s_comb, pair + 1)
                    for s in range(2):
                        done = T.transpose(ps_m1[0:EXPERTS, s * TILE:(s + 1) * TILE], comb_new[:, s, :], ident[0:TILE, 0:TILE])
                    done.then_inc(s_ct, 1)
                down(6)
                if not last:
                    pe.wait_ge(s_cts, pair + 1)
                    for s in range(2):
                        done = T.matmul(nodes(ps_o2)[:, s, :], comb_t[:, s * TILE:(s + 1) * TILE], eb2[:, :], start=True, stop=True)
                    done.then_inc(s_by, 1)
                down(7)

            body(0, True, False)
            with pe.Fori(1, PAIRS) as pair:
                body(pair, False, False)
            body(PAIRS, False, True)

        @block.scalar
        def _(act):
            S = nc.scalar
            act.wait_ge(s_dst, 48)
            act.wait_ge(s_wt, 48)
            act.wait_ge(s_row, 1)
            with act.Fori(0, BLOCKS // 2) as i:
                for u in range(2):
                    cols = ds(i * (2 * BLOCK) + u * BLOCK, BLOCK)
                    act.wait_ge(s_scat[u], i * (16 * BLOCK))
                    S.activation(rec[:, u, :, 0].bitcast(i32), dst_i[:, cols], ACT.Copy).then_inc(s_now, 1)
                    S.activation(rec[:, u, :, 1], row_f[:, cols], ACT.Copy).then_inc(s_now, 1)
                    S.activation(rec[:, u, :, 2], weight[:, cols], ACT.Copy).then_inc(s_now, 1)
                    act.wait_ge(s_slot, i * 2 + u + 1)
                    S.activation(slot_now[:, u, :], slot[:, cols], ACT.Copy).then_inc(s_now, 1)
            act.wait_ge(s_weights, 16 * WEIGHT_LOADS)

            def body(pair, first, last):
                prev = pair - 1

                def gelu(e):
                    if first:
                        return
                    act.wait_ge(s_g, prev * EXPERTS + e + 1)
                    act.wait_ge(s_y, prev * EXPERTS + e)
                    for f in range(KD):
                        S.activation(hid[:, e % 2, f, :], halves(ps_g[e % 2])[:, f, :], ACT.Gelu,
                                     bias=eb1[:, e, f:f + 1]).then_inc(s_gelu, 1)

                gelu(0)
                gelu(1)
                if not last:
                    act.wait_ge(s_h7t, pair + 1)
                    act.wait_ge(s_m1, pair)
                    S.activation(h7_t[:, :, :], halves(ps_tp), ACT.Copy).then_inc(s_h7ts, 1)
                    act.wait_ge(s_m1, pair + 1)
                    act.wait_ge(s_o2, pair)
                    for f in range(KD):
                        S.activation(r1_t[:, f, :], halves(ps_m1)[:, f, :], ACT.Relu, bias=b1_col[:, f:f + 1]).then_inc(s_r1, 1)
                gelu(2)
                gelu(3)
                gelu(4)
                if not last:
                    act.wait_ge(s_tokt, pair + 1)
                    act.wait_ge(s_log, pair)
                    S.activation(tok_new[:, :, :], halves(ps_tp), ACT.Copy).then_inc(s_tokn, 1)
                gelu(5)
                if not last:
                    act.wait_ge(s_shift, pair + 1)
                    act.wait_ge(s_comb, pair)
                    S.activation(expo[:, :, :], shifted[:, :, :], ACT.Exp).then_inc(s_exp, 1)
                gelu(6)
                gelu(7)
                if not last:
                    act.wait_ge(s_ct, pair + 1)
                    act.wait_ge(s_by, pair)
                    S.activation(comb_t[:, :], ps_m1[0:EXPERTS, 0:2 * TILE], ACT.Copy).then_inc(s_cts, 1)
                    act.wait_ge(s_g, pair * EXPERTS)
                    S.activation(tok_t[:, :, :], halves(ps_tp), ACT.Copy).then_inc(s_tokc, 1)

            body(0, True, False)
            with act.Fori(1, PAIRS) as pair:
                body(pair, False, False)
            body(PAIRS, False, True)


_INS = ['x', 'src', 'dst', 'edge_weight', 'L0_gnn_W', 'L0_gnn_b', 'L0_gnn_W1', 'L0_gnn_b1', 'L0_gnn_W2', 'L0_gnn_b2',
        'L0_ffn_router_w', 'L0_ffn_w1', 'L0_ffn_b1', 'L0_ffn_w2', 'L0_ffn_b2']
_OUTS = [((6250, 256), 'float32')]


def kernel(**inputs):
    import numpy as _np
    import concourse.bacc as _bacc
    from concourse import mybir as _mybir
    from concourse.bass_utils import run_bass_kernel_spmd as _run

    nc = _bacc.Bacc("TRN2", target_bir_lowering=False, num_devices=1)
    arrays, args = {}, []
    for name in _INS:
        a = _np.ascontiguousarray(inputs[name])
        arrays[f"in_{name}_dram"] = a
        args.append(nc.dram_tensor(f"in_{name}_dram", a.shape, _mybir.dt.from_np(a.dtype), kind="ExternalInput").ap())
    for i, (shape, dtype) in enumerate(_OUTS):
        dt = _mybir.dt.from_np(_np.dtype(dtype))
        args.append(nc.dram_tensor(f"out_{i}_dram", shape, dt, kind="ExternalOutput").ap())
    build(nc, *args)
    r = _run(nc, [arrays], core_ids=[0])
    return r.results[0]["out_0_dram"]
```
